# Optimizing a Trainium2 kernel written in Bass

```python
import numpy as np
import jax
import jax.numpy as jnp

def _softmax(x, axis=-1):
    return jax.nn.softmax(x, axis=axis)

def _gelu(x):
    return jax.nn.gelu(x, approximate=True)

def _silu(x):
    return jax.nn.silu(x)

def _sigmoid(x):
    return jax.nn.sigmoid(x)

def _layernorm(x, axis=-1, eps=1e-05):
    m = jnp.mean(x, axis=axis, keepdims=True)
    v = jnp.var(x, axis=axis, keepdims=True)
    return (x - m) / jnp.sqrt(v + eps)

def _scatter_add(tgt, idx, src, axis=0):
    return tgt.at[idx].add(src)

def _segment_sum(src, seg, n):
    return jax.ops.segment_sum(src, seg, n)
kernel_name = 'mk_dlrm_tower_d1_rec_r8_ef52c9'

def setup_inputs(seed: int=0):
    np.random.seed(seed)
    _w = jnp.asarray

    def _rec_inputs():
        import jax
        import jax.numpy as jnp
        _tk = jax.random.key(seed)
        ids = jnp.stack([jax.random.randint(jax.random.fold_in(_tk, 200 + f), (512,), 0, v, jnp.int32) for f, v in enumerate([1250, 12500, 12500, 1250, 125000, 12500, 1250, 1250, 1000, 1000, 1000, 12500, 1000, 12500, 12500, 12500, 1250, 1250, 12500, 1250, 1000, 1000, 1000, 1250, 1250, 1000])], axis=1)
        tbl_0 = 0.05 * jax.random.normal(jax.random.fold_in(_tk, 500 + 0), (1250, 128), jnp.float32)
        tbl_1 = 0.05 * jax.random.normal(jax.random.fold_in(_tk, 500 + 1), (12500, 128), jnp.float32)
        tbl_2 = 0.05 * jax.random.normal(jax.random.fold_in(_tk, 500 + 2), (12500, 128), jnp.float32)
        tbl_3 = 0.05 * jax.random.normal(jax.random.fold_in(_tk, 500 + 3), (1250, 128), jnp.float32)
        tbl_4 = 0.05 * jax.random.normal(jax.random.fold_in(_tk, 500 + 4), (125000, 128), jnp.float32)
        tbl_5 = 0.05 * jax.random.normal(jax.random.fold_in(_tk, 500 + 5), (12500, 128), jnp.float32)
        tbl_6 = 0.05 * jax.random.normal(jax.random.fold_in(_tk, 500 + 6), (1250, 128), jnp.float32)
        tbl_7 = 0.05 * jax.random.normal(jax.random.fold_in(_tk, 500 + 7), (1250, 128), jnp.float32)
        tbl_8 = 0.05 * jax.random.normal(jax.random.fold_in(_tk, 500 + 8), (1000, 128), jnp.float32)
        tbl_9 = 0.05 * jax.random.normal(jax.random.fold_in(_tk, 500 + 9), (1000, 128), jnp.float32)
        tbl_10 = 0.05 * jax.random.normal(jax.random.fold_in(_tk, 500 + 10), (1000, 128), jnp.float32)
        tbl_11 = 0.05 * jax.random.normal(jax.random.fold_in(_tk, 500 + 11), (12500, 128), jnp.float32)
        tbl_12 = 0.05 * jax.random.normal(jax.random.fold_in(_tk, 500 + 12), (1000, 128), jnp.float32)
        tbl_13 = 0.05 * jax.random.normal(jax.random.fold_in(_tk, 500 + 13), (12500, 128), jnp.float32)
        tbl_14 = 0.05 * jax.random.normal(jax.random.fold_in(_tk, 500 + 14), (12500, 128), jnp.float32)
        tbl_15 = 0.05 * jax.random.normal(jax.random.fold_in(_tk, 500 + 15), (12500, 128), jnp.float32)
        tbl_16 = 0.05 * jax.random.normal(jax.random.fold_in(_tk, 500 + 16), (1250, 128), jnp.float32)
        tbl_17 = 0.05 * jax.random.normal(jax.random.fold_in(_tk, 500 + 17), (1250, 128), jnp.float32)
        tbl_18 = 0.05 * jax.random.normal(jax.random.fold_in(_tk, 500 + 18), (12500, 128), jnp.float32)
        tbl_19 = 0.05 * jax.random.normal(jax.random.fold_in(_tk, 500 + 19), (1250, 128), jnp.float32)
        tbl_20 = 0.05 * jax.random.normal(jax.random.fold_in(_tk, 500 + 20), (1000, 128), jnp.float32)
        tbl_21 = 0.05 * jax.random.normal(jax.random.fold_in(_tk, 500 + 21), (1000, 128), jnp.float32)
        tbl_22 = 0.05 * jax.random.normal(jax.random.fold_in(_tk, 500 + 22), (1000, 128), jnp.float32)
        tbl_23 = 0.05 * jax.random.normal(jax.random.fold_in(_tk, 500 + 23), (1250, 128), jnp.float32)
        tbl_24 = 0.05 * jax.random.normal(jax.random.fold_in(_tk, 500 + 24), (1250, 128), jnp.float32)
        tbl_25 = 0.05 * jax.random.normal(jax.random.fold_in(_tk, 500 + 25), (1000, 128), jnp.float32)
        _rk = jax.random.fold_in(_tk, 7)
        r_dense_x = -0.000514642 + 1.00011 * jax.random.normal(jax.random.fold_in(_rk, 101), (512, 128), jnp.float32)
        W_top1 = 0.0456912 * jax.random.normal(jax.random.fold_in(_tk, 801), (479, 512), jnp.float32)
        W_top2 = 0.0441942 * jax.random.normal(jax.random.fold_in(_tk, 802), (512, 256), jnp.float32)
        W_top3 = 0.0625 * jax.random.normal(jax.random.fold_in(_tk, 803), (256, 1), jnp.float32)
        b_top1 = jnp.zeros((512,), jnp.float32)
        b_top2 = jnp.zeros((256,), jnp.float32)
        return (r_dense_x, ids, tbl_0, tbl_1, tbl_2, tbl_3, tbl_4, tbl_5, tbl_6, tbl_7, tbl_8, tbl_9, tbl_10, tbl_11, tbl_12, tbl_13, tbl_14, tbl_15, tbl_16, tbl_17, tbl_18, tbl_19, tbl_20, tbl_21, tbl_22, tbl_23, tbl_24, tbl_25, W_top1, b_top1, W_top2, b_top2, W_top3)
    r_dense_x, ids, tbl_0, tbl_1, tbl_2, tbl_3, tbl_4, tbl_5, tbl_6, tbl_7, tbl_8, tbl_9, tbl_10, tbl_11, tbl_12, tbl_13, tbl_14, tbl_15, tbl_16, tbl_17, tbl_18, tbl_19, tbl_20, tbl_21, tbl_22, tbl_23, tbl_24, tbl_25, W_top1, b_top1, W_top2, b_top2, W_top3 = _rec_inputs()

    def _L0_rec_setup():
        import jax, jax.numpy as jnp
        import numpy as np
        F = 26
        D = 128
        B = 2048
        _TRIU_I, _TRIU_J = np.triu_indices(F + 1, k=1)
        _TRIU_I = jnp.asarray(_TRIU_I)
        _TRIU_J = jnp.asarray(_TRIU_J)
        key = jax.random.key(seed)
        k1, k2 = jax.random.split(key)
        sparse_x = jax.random.normal(k1, (B, F, D), dtype=jnp.float32)
        dense_x = jax.random.normal(k2, (B, D), dtype=jnp.float32)
        return {'sparse_x': sparse_x, 'dense_x': dense_x}
    _L0_rec_all = _L0_rec_setup()
    _L0_rec_in = {k: v for k, v in _L0_rec_all.items() if k in ()}
    del _L0_rec_all
    return {'r_dense_x': r_dense_x, 'ids': ids, 'tbl_0': tbl_0, 'tbl_1': tbl_1, 'tbl_2': tbl_2, 'tbl_3': tbl_3, 'tbl_4': tbl_4, 'tbl_5': tbl_5, 'tbl_6': tbl_6, 'tbl_7': tbl_7, 'tbl_8': tbl_8, 'tbl_9': tbl_9, 'tbl_10': tbl_10, 'tbl_11': tbl_11, 'tbl_12': tbl_12, 'tbl_13': tbl_13, 'tbl_14': tbl_14, 'tbl_15': tbl_15, 'tbl_16': tbl_16, 'tbl_17': tbl_17, 'tbl_18': tbl_18, 'tbl_19': tbl_19, 'tbl_20': tbl_20, 'tbl_21': tbl_21, 'tbl_22': tbl_22, 'tbl_23': tbl_23, 'tbl_24': tbl_24, 'tbl_25': tbl_25, 'W_top1': W_top1, 'b_top1': b_top1, 'W_top2': W_top2, 'b_top2': b_top2, 'W_top3': W_top3}

def reference(r_dense_x, ids, tbl_0, tbl_1, tbl_2, tbl_3, tbl_4, tbl_5, tbl_6, tbl_7, tbl_8, tbl_9, tbl_10, tbl_11, tbl_12, tbl_13, tbl_14, tbl_15, tbl_16, tbl_17, tbl_18, tbl_19, tbl_20, tbl_21, tbl_22, tbl_23, tbl_24, tbl_25, W_top1, b_top1, W_top2, b_top2, W_top3):
    import jax
    import jax.numpy as jnp

    def _L0_rec_ref(sparse_x, dense_x):
        import jax, jax.numpy as jnp
        import numpy as np
        F = 26
        D = 128
        B = 2048
        _TRIU_I, _TRIU_J = np.triu_indices(F + 1, k=1)
        _TRIU_I = jnp.asarray(_TRIU_I)
        _TRIU_J = jnp.asarray(_TRIU_J)
        combined = jnp.concatenate([sparse_x, dense_x[:, None, :]], axis=1)
        interact = jnp.einsum('bfd,bgd->bfg', combined, combined)
        return interact[:, _TRIU_I, _TRIU_J]
    e = jnp.stack([tbl_0[ids[:, 0]], tbl_1[ids[:, 1]], tbl_2[ids[:, 2]], tbl_3[ids[:, 3]], tbl_4[ids[:, 4]], tbl_5[ids[:, 5]], tbl_6[ids[:, 6]], tbl_7[ids[:, 7]], tbl_8[ids[:, 8]], tbl_9[ids[:, 9]], tbl_10[ids[:, 10]], tbl_11[ids[:, 11]], tbl_12[ids[:, 12]], tbl_13[ids[:, 13]], tbl_14[ids[:, 14]], tbl_15[ids[:, 15]], tbl_16[ids[:, 16]], tbl_17[ids[:, 17]], tbl_18[ids[:, 18]], tbl_19[ids[:, 19]], tbl_20[ids[:, 20]], tbl_21[ids[:, 21]], tbl_22[ids[:, 22]], tbl_23[ids[:, 23]], tbl_24[ids[:, 24]], tbl_25[ids[:, 25]]], axis=1)
    z = _L0_rec_ref(e, r_dense_x)
    z = z.reshape(z.shape[0], -1)
    h = jnp.concatenate([z, r_dense_x], axis=1)
    h = jnp.maximum(h @ W_top1 + b_top1, 0.0)
    h = jnp.maximum(h @ W_top2 + b_top2, 0.0)
    y = h @ W_top3
    return y

_drawn_inputs = setup_inputs


def setup_inputs(seed=0):
    import zlib

    import numpy as np

    out = dict(_drawn_inputs(seed))
    spreads = {'b_top1': (0.0, 0.1), 'b_top2': (0.0, 0.1)}
    factors = {}
    for name, (base, spread) in spreads.items():
        noise = np.random.default_rng([zlib.crc32(name.encode()), seed]).standard_normal(out[name].shape)
        drawn = base * np.exp(spread * noise) if base else spread * noise
        out[name] = jnp.asarray(drawn.astype(out[name].dtype))
    for name, factor in factors.items():
        out[name] = (out[name] * factor).astype(out[name].dtype)
    return out
```

```python
from contextlib import ExitStack

import concourse.bass as bass
from concourse import mybir

F32 = mybir.dt.float32
I32 = mybir.dt.int32
ALU = mybir.AluOpType
ACT = mybir.ActivationFunctionType

P = 128
D = 128
BATCH = 512
TABLES = 26
VECTORS = TABLES + 1
DENSE = TABLES
TILES = BATCH // P
QUADS = 4
ROWS = P // QUADS
PER = 7
COLS = QUADS * PER
GROUP = QUADS
GROUPS = P // GROUP
BANK = 512
GPB = BANK // (GROUP * COLS)
UNIT_BANKS = 2
GPU = GPB * UNIT_BANKS
UNITS = GROUPS // GPU
CHUNK = BANK // P
CHUNKS = -(-VECTORS // CHUNK)
H1, H2 = 512, 256
N1, N2 = H1 // P, H2 // P


def pair_row(i, j):
    i, j = min(i, j), max(i, j)
    return i * VECTORS - i * (i + 1) // 2 + j - i - 1


def build(nc, r_dense_x, ids, tables, w1_pairs, w1_dense, w2, w3, b1, b2, out):
    with ExitStack() as ctx:
        def sb(name, shape, dt=F32):
            return ctx.enter_context(nc.sbuf_tensor(name, shape, dt))

        def psum(name, shape):
            return ctx.enter_context(nc.psum_tensor(name, shape, F32))

        def sem(name):
            return ctx.enter_context(nc.semaphore(name))

        ids_sb = sb("ids_sb", [P, TILES, TABLES], I32)
        rows = sb("rows", [P, TILES, VECTORS, D])
        xt = sb("xt", [P, BATCH, ROWS])
        z = sb("z", [P, TILES, PER, P])
        w1p_sb = sb("w1p_sb", [P, PER, H1])
        w1d_sb = sb("w1d_sb", [P, H1])
        w2_sb = sb("w2_sb", [P, N1, H2])
        w3_sb = sb("w3_sb", [P, N2])
        b1_sb = sb("b1_sb", [P, N1])
        b2_sb = sb("b2_sb", [P, N2])
        h1 = sb("h1", [P, 2, N1, P])
        h2 = sb("h2", [P, 2, N2, P])
        y = sb("y", [1, BATCH])
        ident = sb("ident", [P, P])

        ps_t = psum("ps_t", [P, 2, BANK])
        ps_g = psum("ps_g", [P, 2, UNIT_BANKS, BANK])
        ps_m = psum("ps_m", [P, 2, BANK])

        ids_landed = sem("ids_landed")
        dense_landed = sem("dense_landed")
        w1_landed = sem("w1_landed")
        w23_landed = sem("w23_landed")
        biases_landed = sem("biases_landed")
        rows_landed = [[sem(f"rows_landed_{t}_{c}") for c in range(CHUNKS)] for t in range(TILES)]
        ident_zeroed = sem("ident_zeroed")
        ident_ready = sem("ident_ready")
        pads_zeroed = sem("pads_zeroed")
        transposed = sem("transposed")
        xt_dve = sem("xt_dve")
        xt_act = sem("xt_act")
        gram_done = sem("gram_done")
        z_dve = sem("z_dve")
        z_act = sem("z_act")
        l1_done = sem("l1_done")
        h1_dve = sem("h1_dve")
        h1_act = sem("h1_act")
        l2_done = sem("l2_done")
        h2_act = sem("h2_act")
        l3_done = sem("l3_done")
        y_dve = sem("y_dve")
        y_stored = sem("y_stored")

        def chunk_slots(c):
            return range(c * CHUNK, min((c + 1) * CHUNK, VECTORS))

        def chunks_before(t, parity):
            return len([k for k in range(t * CHUNKS) if k % 2 == parity])

        def move_chunk(copy, k):
            t, c = divmod(k, CHUNKS)
            s = chunk_slots(c)
            src = ps_t[:, k % 2, 0:len(s) * P].rearrange("d (s b) -> d b s", b=P)
            return copy(xt[:, t * P:(t + 1) * P, s.start:s.stop], src)

        def move_gram(copy, n, quads):
            t, u = divmod(n, UNITS)
            for q in quads:
                for r in range(QUADS):
                    src = ps_g[ROWS * q:ROWS * (q + 1), n % 2, :, 0:GPB * GROUP * COLS].rearrange(
                        "p k (g m) -> p k g m", g=GPB)[:, :, :, q * COLS + r * PER:q * COLS + (r + 1) * PER]
                    lo = q * GROUPS + u * GPU
                    dst = z[ROWS * r:ROWS * (r + 1), t, :, lo:lo + GPU].rearrange("p c (k g) -> p k g c", k=UNIT_BANKS)
                    last = copy(dst, src)
            return last

        block = ctx.enter_context(nc.Block())

        @block.sync
        def _(sp):
            sp.dma_start(ids_sb[:], ids.rearrange("(t p) f -> p t f", p=P)).then_inc(ids_landed, 16)
            sp.dma_start(rows[:, :, DENSE, :], r_dense_x.rearrange("(t p) d -> p t d", p=P)).then_inc(dense_landed, 16)
            sp.dma_start(w1d_sb[:], w1_dense).then_inc(w1_landed, 16)
            sp.dma_start(w1p_sb[:], w1_pairs).then_inc(w1_landed, 16)
            sp.dma_start(w2_sb[:], w2.rearrange("(k p) n -> p k n", p=P)).then_inc(w23_landed, 16)
            sp.dma_start(w3_sb[:], w3).then_inc(w23_landed, 16)
            sp.dma_start(b1_sb[:], b1).then_inc(biases_landed, 16)
            sp.dma_start(b2_sb[:], b2).then_inc(biases_landed, 16)
            sp.wait_ge(y_dve, TILES)
            sp.dma_start(out, y[:]).then_inc(y_stored, 16)
            sp.wait_ge(y_stored, 16)

        @block.gpsimd
        def _(pool):
            pool.memset(ident[:], 0.0).then_inc(ident_zeroed, 1)
            pool.wait_ge(ident_zeroed, 1)
            pool.affine_select(out=ident[:], in_=ident[:], compare_op=ALU.not_equal, fill=1.0, base=0,
                               pattern=[[-1, P]], channel_multiplier=1).then_inc(ident_ready, 1)
            pool.wait_ge(ids_landed, 16)
            for t in range(TILES):
                for c in range(CHUNKS):
                    for f in chunk_slots(c):
                        if f != DENSE:
                            pool.indirect_dma_start(
                                out=rows[:, t, f, :], out_offset=None, in_=tables[f],
                                in_offset=bass.IndirectOffsetOnAxis(ap=ids_sb[:, t, f:f + 1], axis=0),
                            ).then_inc(rows_landed[t][c], 16)

        @block.tensor
        def _(pe):
            pe.wait_ge(ident_ready, 1)
            for t in range(TILES):
                for c in range(CHUNKS):
                    k = t * CHUNKS + c
                    s = chunk_slots(c)
                    pe.wait_ge(rows_landed[t][c], 16 * len([f for f in s if f != DENSE]))
                    if DENSE in s:
                        pe.wait_ge(dense_landed, 16)
                    if k >= 2:
                        pe.wait_ge(xt_act if k % 2 else xt_dve, k // 2)
                    for i, f in enumerate(s):
                        last = pe.transpose(ps_t[:, k % 2, i * P:(i + 1) * P], rows[:, t, f, :], ident[:])
                    last.then_inc(transposed, 1)
                pe.wait_ge(pads_zeroed, 1)
                pe.wait_ge(xt_dve, chunks_before(t + 1, 0))
                pe.wait_ge(xt_act, chunks_before(t + 1, 1))
                for u in range(UNITS):
                    n = t * UNITS + u
                    if n >= 2:
                        pe.wait_ge(z_dve, n - 1)
                        pe.wait_ge(z_act, n - 1)
                    for g in range(GPU):
                        b = t * P + (u * GPU + g) * GROUP
                        at = (g % GPB) * GROUP * COLS
                        last = pe.matmul(ps_g[:, n % 2, g // GPB, at:at + GROUP * COLS],
                                         xt[:, b:b + GROUP, :], xt[:, b:b + GROUP, 0:COLS], start=True, stop=True)
                    last.then_inc(gram_done, 1)
                if t == 0:
                    pe.wait_ge(w1_landed, 32)
                if t >= 1:
                    pe.wait_ge(h2_act, t)
                    pe.wait_ge(y_dve, t)
                pe.wait_ge(z_dve, (t + 1) * UNITS)
                pe.wait_ge(z_act, (t + 1) * UNITS)
                dense = xt[:, t * P:(t + 1) * P, DENSE].rearrange("d (g q) -> d q g", q=GROUP)
                for n in range(N1):
                    dst = ps_m[:, n // 2, (n % 2) * P:(n % 2 + 1) * P]
                    pe.matmul(dst, w1d_sb[:, n * P:(n + 1) * P], dense, start=True, stop=False)
                    for c in range(PER):
                        last = pe.matmul(dst, w1p_sb[:, c, n * P:(n + 1) * P], z[:, t, c, :],
                                         start=False, stop=(c == PER - 1))
                    if n % 2:
                        last.then_inc(l1_done, 1)
                if t == 0:
                    pe.wait_ge(w23_landed, 32)
                pe.wait_ge(h1_dve, t + 1)
                pe.wait_ge(h1_act, t + 1)
                for m in range(N2):
                    for n in range(N1):
                        last = pe.matmul(ps_m[:, 0, m * P:(m + 1) * P], w2_sb[:, n, m * P:(m + 1) * P],
                                         h1[:, t % 2, n, :], start=(n == 0), stop=(n == N1 - 1))
                last.then_inc(l2_done, 1)
                pe.wait_ge(h2_act, t + 1)
                for m in range(N2):
                    last = pe.matmul(ps_m[0:1, 1, 0:P], w3_sb[:, m:m + 1], h2[:, t % 2, m, :],
                                     start=(m == 0), stop=(m == N2 - 1))
                last.then_inc(l3_done, 1)

        @block.vector
        def _(dve):
            dve.memset(xt[:, :, VECTORS:ROWS], 0.0).then_inc(pads_zeroed, 1)
            for t in range(TILES):
                for k in range(t * CHUNKS, (t + 1) * CHUNKS):
                    if k % 2 == 0:
                        dve.wait_ge(transposed, k + 1)
                        move_chunk(dve.tensor_copy, k).then_inc(xt_dve, 1)
                for n in range(t * UNITS, (t + 1) * UNITS):
                    dve.wait_ge(gram_done, n + 1)
                    move_gram(dve.tensor_copy, n, (0, 1)).then_inc(z_dve, 1)
                if t == 0:
                    dve.wait_ge(biases_landed, 32)
                dve.wait_ge(l1_done, 2 * t + 1)
                for n in range(N1 // 2):
                    last = dve.tensor_scalar(h1[:, t % 2, n, :], ps_m[:, 0, n * P:(n + 1) * P],
                                             b1_sb[:, n:n + 1], 0.0, ALU.add, ALU.max)
                last.then_inc(h1_dve, 1)
                dve.wait_ge(l3_done, t + 1)
                dve.tensor_copy(y[0:1, t * P:(t + 1) * P].rearrange("p (g q) -> p q g", q=GROUP),
                                ps_m[0:1, 1, 0:P].rearrange("p (q g) -> p q g", q=GROUP)).then_inc(y_dve, 1)

        @block.scalar
        def _(act):
            for t in range(TILES):
                for k in range(t * CHUNKS, (t + 1) * CHUNKS):
                    if k % 2 == 1:
                        act.wait_ge(transposed, k + 1)
                        move_chunk(act.copy, k).then_inc(xt_act, 1)
                for n in range(t * UNITS, (t + 1) * UNITS):
                    act.wait_ge(gram_done, n + 1)
                    move_gram(act.copy, n, (2, 3)).then_inc(z_act, 1)
                if t == 0:
                    act.wait_ge(biases_landed, 32)
                act.wait_ge(l1_done, 2 * t + 2)
                for n in range(N1 // 2, N1):
                    last = act.activation(h1[:, t % 2, n, :], ps_m[:, 1, (n % 2) * P:(n % 2 + 1) * P],
                                          ACT.Relu, bias=b1_sb[:, n:n + 1])
                last.then_inc(h1_act, 1)
                act.wait_ge(l2_done, t + 1)
                for m in range(N2):
                    last = act.activation(h2[:, t % 2, m, :], ps_m[:, 0, m * P:(m + 1) * P],
                                          ACT.Relu, bias=b2_sb[:, m:m + 1])
                last.then_inc(h2_act, 1)


def kernel(**inputs):
    import numpy as np
    import concourse.bacc as bacc
    from concourse.bass_utils import run_bass_kernel_spmd

    w1 = np.asarray(inputs["W_top1"])
    pairs = VECTORS * (VECTORS - 1) // 2
    w1_pairs = np.zeros((P, PER, H1), w1.dtype)
    for column in range(VECTORS):
        for i in range(column + 1, VECTORS):
            w1_pairs[ROWS * (column // PER) + i, column % PER] = w1[pair_row(column, i)]
    arrays = {
        "r_dense_x": np.asarray(inputs["r_dense_x"]),
        "ids": np.asarray(inputs["ids"]),
        **{f"tbl_{f}": np.asarray(inputs[f"tbl_{f}"]) for f in range(TABLES)},
        "w1_pairs": w1_pairs,
        "w1_dense": w1[pairs:],
        "w2": np.asarray(inputs["W_top2"]),
        "w3": np.asarray(inputs["W_top3"]).reshape(N2, P).T,
        "b1": np.asarray(inputs["b_top1"]).reshape(N1, P).T,
        "b2": np.asarray(inputs["b_top2"]).reshape(N2, P).T,
    }
    arrays = {f"{name}_dram": np.ascontiguousarray(a) for name, a in arrays.items()}

    nc = bacc.Bacc("TRN2", target_bir_lowering=False, num_devices=1)
    aps = {name: nc.dram_tensor(name, a.shape, mybir.dt.from_np(a.dtype), kind="ExternalInput").ap()
           for name, a in arrays.items()}
    out = nc.dram_tensor("out_dram", (1, BATCH), F32, kind="ExternalOutput").ap()
    build(nc, aps["r_dense_x_dram"], aps["ids_dram"], [aps[f"tbl_{f}_dram"] for f in range(TABLES)],
          aps["w1_pairs_dram"], aps["w1_dense_dram"], aps["w2_dram"], aps["w3_dram"],
          aps["b1_dram"], aps["b2_dram"], out)
    result = run_bass_kernel_spmd(nc, [arrays], core_ids=[0])
    return result.results[0]["out_dram"].reshape(BATCH, 1)
```

```python
from contextlib import ExitStack

import concourse.bass as bass
from concourse import mybir

F32 = mybir.dt.float32
F32R = mybir.dt.float32r
I32 = mybir.dt.int32
ALU = mybir.AluOpType
ACT = mybir.ActivationFunctionType

P = 128
D = 128
BATCH = 512
TABLES = 26
VECTORS = TABLES + 1
HOT_ROWS = 1000
HOT = 6
HOT_CHUNKS = 8
HOT_P = HOT_ROWS // HOT_CHUNKS
HOT_DVE = 5
HOT_ACT = HOT_CHUNKS - HOT_DVE
HOT_ORDER = (0, 1, 5, 2, 3, 6, 4, 7)
GATHERED = TABLES - HOT
DENSE = 0
FIRST_HOT = 1 + GATHERED
WARM_UP = 5
TILES = BATCH // P
QUADS = 4
ROWS = P // QUADS
PER = -(-VECTORS // QUADS)
COLS = PER * QUADS
FOLDS = PER // 2
FOLDED = PER - FOLDS
GROUP = QUADS
GROUPS = P // GROUP
BANK = 512
GPB = BANK // (GROUP * COLS)
UNIT_BANKS = 2
GPU = GPB * UNIT_BANKS
UNITS = GROUPS // GPU
CHUNK = BANK // P
CHUNKS = -(-(FIRST_HOT) // CHUNK)
TRANSPOSES = ((0, 1, 2, 3, 3, CHUNKS), (0, 1, 2, 3, 3, CHUNKS), (0, 0, 1, 2, 2, CHUNKS))
H1, H2 = 512, 256
N1, N2 = H1 // P, H2 // P
L2_ORDER = (0, 2, 1, 3)


def pair_row(i, j):
    i, j = min(i, j), max(i, j)
    return i * VECTORS - i * (i + 1) // 2 + j - i - 1


def labels_of_slots():
    labels, firsts, half = {}, 0, VECTORS // 2
    for r in range(QUADS):
        for c in range(FOLDS):
            first, second = PER * r + c, PER * r + c + FOLDED
            if second < VECTORS:
                labels[first], labels[second] = firsts, firsts + half
                firsts += 1
    others = [x for x in range(VECTORS) if x not in labels.values()]
    for s in range(VECTORS):
        if s not in labels:
            labels[s] = others.pop(0)
    return labels


def takes(labels, row, column):
    return column < VECTORS and 1 <= (labels[column] - labels[row]) % VECTORS <= VECTORS // 2


def slot_tables(row_counts):
    hot = [f for f, rows in enumerate(row_counts) if rows == HOT_ROWS][:HOT]
    return [f for f in range(TABLES) if f not in hot], hot


def build(nc, r_dense_x, ids, hot_ids, codes, second, gathered_tables, hot_tables, w1_pairs, w1_dense, w2, w3, b1, b2, out):
    with ExitStack() as ctx:
        def sb(name, shape, dt=F32):
            return ctx.enter_context(nc.sbuf_tensor(name, shape, dt))

        def psum(name, shape):
            return ctx.enter_context(nc.psum_tensor(name, shape, F32))

        def sem(name):
            return ctx.enter_context(nc.semaphore(name))

        ids_sb = sb("ids_sb", [P, TILES, GATHERED], I32)
        hot_ids_sb = sb("hot_ids_sb", [HOT, BATCH], I32)
        hot_ids_r = sb("hot_ids_r", [HOT, BATCH], F32R)
        select = sb("select", [HOT, HOT, HOT_P], F32R)
        codes_sb = sb("codes_sb", [HOT_P, 2, HOT_CHUNKS])
        table = sb("table", [HOT_P, 2, HOT_CHUNKS * D])
        hi = sb("hi", [HOT_P, 2, HOT_CHUNKS * D], F32R)
        lo = sb("lo", [HOT_P, 2, HOT_CHUNKS * D], F32R)
        onehot = sb("onehot", [HOT_P, 2, HOT_CHUNKS, BATCH], F32R)
        distance = sb("distance", [HOT_P, 2, BATCH])
        rows = sb("rows", [P, TILES, FIRST_HOT, D])
        xt = sb("xt", [P, BATCH, ROWS])
        z = sb("z", [P, 2, PER, P])
        second_sb = sb("second_sb", [P, FOLDS], I32)
        w1p_sb = sb("w1p_sb", [P, FOLDED, H1])
        w1d_sb = sb("w1d_sb", [P, H1])
        w2_sb = sb("w2_sb", [P, N1, H2])
        w3_sb = sb("w3_sb", [P, N2])
        b1_sb = sb("b1_sb", [P, N1])
        b2_sb = sb("b2_sb", [P, N2])
        h1 = sb("h1", [P, N1, P])
        h2 = sb("h2", [P, N2, P])
        y = sb("y", [1, BATCH])
        ident = sb("ident", [P, P])

        ps_t = psum("ps_t", [P, 2, BANK])
        ps_g = psum("ps_g", [P, 2, UNIT_BANKS, BANK])
        ps_m = psum("ps_m", [P, 2, BANK])

        ids_landed = sem("ids_landed")
        hot_ids_landed = sem("hot_ids_landed")
        codes_landed = sem("codes_landed")
        table_landed = [sem(f"table_landed_{i}") for i in range(2)]
        hot_ids_ready = sem("hot_ids_ready")
        select_ready = sem("select_ready")
        hi_ready = sem("hi_ready")
        lo_ready = sem("lo_ready")
        ids_spread = sem("ids_spread")
        hot_dve = sem("hot_dve")
        hot_act = sem("hot_act")
        distances = sem("distances")
        looked_up = sem("looked_up")
        xt_hot = sem("xt_hot")
        dense_landed = sem("dense_landed")
        w1_landed = sem("w1_landed")
        w23_landed = sem("w23_landed")
        biases_landed = sem("biases_landed")
        second_landed = sem("second_landed")
        rows_landed = [[sem(f"rows_landed_{t}_{c}") for c in range(CHUNKS)] for t in range(TILES)]
        ident_zeroed = sem("ident_zeroed")
        ident_ready = sem("ident_ready")
        pads_zeroed = sem("pads_zeroed")
        transposed = sem("transposed")
        xt_dve = sem("xt_dve")
        xt_act = sem("xt_act")
        gram_done = sem("gram_done")
        z_dve = sem("z_dve")
        z_act = sem("z_act")
        folded = sem("folded")
        l1_done = sem("l1_done")
        h1_dve = sem("h1_dve")
        h1_act = sem("h1_act")
        l2_done = sem("l2_done")
        h2_act = sem("h2_act")
        l3_done = sem("l3_done")
        y_dve = sem("y_dve")
        y_stored = sem("y_stored")

        def chunk_slots(c):
            return range(c * CHUNK, min((c + 1) * CHUNK, FIRST_HOT))

        def chunks_before(t, parity):
            return len([k for k in range(t * CHUNKS) if k % 2 == parity])

        def move_chunk(copy, k):
            t, c = divmod(k, CHUNKS)
            s = chunk_slots(c)
            src = ps_t[:, k % 2, 0:len(s) * P].rearrange("d (s b) -> d b s", b=P)
            return copy(xt[:, t * P:(t + 1) * P, s.start:s.stop], src)

        def move_gram(copy, n, quads):
            t, u = divmod(n, UNITS)
            for q in quads:
                for r in range(QUADS):
                    src = ps_g[ROWS * q:ROWS * (q + 1), n % 2, :, 0:GPB * GROUP * COLS].rearrange(
                        "p k (g m) -> p k g m", g=GPB)[:, :, :, q * COLS + r * PER:q * COLS + (r + 1) * PER]
                    first = q * GROUPS + u * GPU
                    dst = z[ROWS * r:ROWS * (r + 1), t % 2, :, first:first + GPU].rearrange("p c (k g) -> p k g c", k=UNIT_BANKS)
                    last = copy(dst, src)
            return last

        def l1_block(n):
            return ps_m[:, n % 2, (n // 2) * P:(n // 2 + 1) * P]

        def l2_block(m):
            return ps_m[:, m, (N1 // 2) * P:(N1 // 2 + 1) * P]

        l3_row = ps_m[0:1, 0, BANK - P:BANK]

        def transposes_after(t, step):
            chunks = range(max((t + 1) * CHUNKS, HOT), min((t + 2) * CHUNKS, TILES * CHUNKS))
            steps = ("unit 0", "unit 1", "unit 2", "unit 3", "layer 1", "layer 2")
            ends = TRANSPOSES[t] if t < len(TRANSPOSES) else (0,) * len(steps)
            at = steps.index(step)
            return chunks[ends[at - 1] if at else 0:ends[at]]

        block = ctx.enter_context(nc.Block())

        @block.sync
        def _(sp):
            def load_table(i):
                src = hot_tables[i].rearrange("(p c) d -> p (c d)", c=HOT_CHUNKS)
                if i >= 2:
                    sp.wait_ge(lo_ready, i - 1)
                whole = HOT_P // 16 * 16
                sp.dma_start(table[0:whole, i % 2, :], src[0:whole]).then_inc(table_landed[i % 2], 16)
                sp.dma_start(table[whole:HOT_P, i % 2, :], src[whole:HOT_P]).then_inc(table_landed[i % 2], 16)

            sp.dma_start(hot_ids_sb[:], hot_ids).then_inc(hot_ids_landed, 16)
            load_table(0)
            load_table(1)
            sp.dma_start(rows[:, :, DENSE, :], r_dense_x.rearrange("(t p) d -> p t d", p=P)).then_inc(dense_landed, 16)
            for i in range(2, HOT):
                load_table(i)
            sp.dma_start(second_sb[:], second).then_inc(second_landed, 16)
            sp.dma_start(w1d_sb[:], w1_dense).then_inc(w1_landed, 16)
            sp.dma_start(w1p_sb[:], w1_pairs).then_inc(w1_landed, 16)
            sp.dma_start(w2_sb[:], w2.rearrange("(k p) n -> p k n", p=P)).then_inc(w23_landed, 16)
            sp.dma_start(w3_sb[:], w3).then_inc(w23_landed, 16)
            sp.dma_start(b1_sb[:], b1).then_inc(biases_landed, 16)
            sp.dma_start(b2_sb[:], b2).then_inc(biases_landed, 16)
            sp.wait_ge(y_dve, TILES)
            sp.dma_start(out, y[:]).then_inc(y_stored, 16)
            sp.wait_ge(y_stored, 16)

        @block.gpsimd
        def _(pool):
            pool.memset(ident[:], 0.0).then_inc(ident_zeroed, 1)
            pool.wait_ge(ident_zeroed, 1)
            pool.affine_select(out=ident[:], in_=ident[:], compare_op=ALU.not_equal, fill=1.0, base=0,
                               pattern=[[-1, P]], channel_multiplier=1).then_inc(ident_ready, 1)
            pool.wait_ge(ids_landed, 16)
            for t in range(TILES):
                for c in range(CHUNKS):
                    for f in chunk_slots(c):
                        if f != DENSE:
                            pool.indirect_dma_start(
                                out=rows[:, t, f, :], out_offset=None, in_=gathered_tables[f - 1],
                                in_offset=bass.IndirectOffsetOnAxis(ap=ids_sb[:, t, f - 1:f], axis=0),
                            ).then_inc(rows_landed[t][c], 16)

        @block.tensor
        def _(pe):
            def spread_ids(i):
                for e in range(2):
                    last = pe.matmul(ps_g[0:HOT_P, e, i % 2, :], select[:, i, :], hot_ids_r[:], start=True, stop=True)
                last.then_inc(ids_spread, 1)

            def look_up(i):
                pe.wait_ge(hi_ready, i + 1)
                if i >= 2:
                    pe.wait_ge(xt_hot, i - 1)
                order = [(c, half) for c in HOT_ORDER for half in (hi, lo)] if i else \
                        [(c, half) for half in (hi, lo) for c in HOT_ORDER]
                for step, (c, half) in enumerate(order):
                    if half is hi:
                        if c < HOT_DVE:
                            pe.wait_ge(hot_dve, i * HOT_DVE + c + 1)
                        else:
                            pe.wait_ge(hot_act, i * HOT_ACT + c - HOT_DVE + 1)
                    elif c == HOT_ORDER[0]:
                        pe.wait_ge(lo_ready, i + 1)
                    last = pe.matmul(ps_m[:, i % 2, :], half[:, i % 2, c * D:(c + 1) * D], onehot[:, i % 2, c, :],
                                     start=(step == 0), stop=(step == len(order) - 1))
                last.then_inc(looked_up, 1)

            def layer_3(t):
                for m in range(N2):
                    pe.wait_ge(h2_act, t * N2 + m + 1)
                    last = pe.matmul(l3_row, w3_sb[:, m:m + 1], h2[:, m, :],
                                     start=(m == 0), stop=(m == N2 - 1))
                last.then_inc(l3_done, 1)

            def transpose_chunk(k):
                t, c = divmod(k, CHUNKS)
                s = chunk_slots(c)
                pe.wait_ge(rows_landed[t][c], 16 * len([f for f in s if f != DENSE]))
                if DENSE in s:
                    pe.wait_ge(dense_landed, 16)
                if k >= 2:
                    pe.wait_ge(xt_act if k % 2 else xt_dve, k // 2)
                for i, f in enumerate(s):
                    last = pe.transpose(ps_t[:, k % 2, i * P:(i + 1) * P], rows[:, t, f, :], ident[:])
                last.then_inc(transposed, 1)

            pe.wait_ge(ident_ready, 1)
            for _ in range(WARM_UP):
                pe.matmul(ps_t[:, 0, 0:P], ident[:], ident[:], start=True, stop=True)
            pe.wait_ge(hot_ids_ready, 1)
            pe.wait_ge(select_ready, 1)
            spread_ids(0)
            spread_ids(1)
            for i in range(HOT):
                look_up(i)
                if i + 2 < HOT:
                    spread_ids(i + 2)
                transpose_chunk(i)
            for t in range(TILES):
                pe.wait_ge(pads_zeroed, 1 + t // 2)
                pe.wait_ge(xt_hot, HOT)
                pe.wait_ge(xt_dve, chunks_before(t + 1, 0))
                pe.wait_ge(xt_act, chunks_before(t + 1, 1))
                for u in range(UNITS):
                    n = t * UNITS + u
                    if n >= 2:
                        pe.wait_ge(z_dve, n - 1)
                        pe.wait_ge(z_act, n - 1)
                    for g in range(GPU):
                        b = t * P + (u * GPU + g) * GROUP
                        at = (g % GPB) * GROUP * COLS
                        last = pe.matmul(ps_g[:, n % 2, g // GPB, at:at + GROUP * COLS],
                                         xt[:, b:b + GROUP, :], xt[:, b:b + GROUP, 0:COLS], start=True, stop=True)
                    last.then_inc(gram_done, 1)
                    if u == 0 and t >= 1:
                        layer_3(t - 1)
                    for k in transposes_after(t, f"unit {u}"):
                        transpose_chunk(k)
                if t == 0:
                    pe.wait_ge(w1_landed, 32)
                if t >= 1:
                    pe.wait_ge(h2_act, t * N2)
                    pe.wait_ge(y_dve, t)
                dense = xt[:, t * P:(t + 1) * P, DENSE].rearrange("d (g q) -> d q g", q=GROUP)
                for n in range(N1):
                    for first in ((0, 1), (), (2,), (3,))[n]:
                        if first == 2:
                            pe.wait_ge(h1_dve, t * 2 + 1)
                        if first == 3:
                            pe.wait_ge(h1_act, t * 2 + 1)
                        pe.matmul(l1_block(first), w1d_sb[:, first * P:(first + 1) * P], dense, start=True, stop=False)
                    if n == 0:
                        pe.wait_ge(folded, (t + 1) * UNITS)
                    for c in range(FOLDED):
                        last = pe.matmul(l1_block(n), w1p_sb[:, c, n * P:(n + 1) * P], z[:, t % 2, c, :],
                                         start=False, stop=(c == FOLDED - 1))
                    last.then_inc(l1_done, 1)
                for k in transposes_after(t, "layer 1"):
                    transpose_chunk(k)
                if t == 0:
                    pe.wait_ge(w23_landed, 32)
                pe.wait_ge(h1_dve, (t + 1) * 2)
                for m in range(N2):
                    for n in L2_ORDER:
                        if m == 0 and n == L2_ORDER[-1]:
                            pe.wait_ge(h1_act, (t + 1) * 2)
                        last = pe.matmul(l2_block(m), w2_sb[:, n, m * P:(m + 1) * P],
                                         h1[:, n, :], start=(n == 0), stop=(n == L2_ORDER[-1]))
                    last.then_inc(l2_done, 1)
                for k in transposes_after(t, "layer 2"):
                    transpose_chunk(k)
            layer_3(TILES - 1)

        @block.vector
        def _(dve):
            def move_chunks(chunks):
                for k in chunks:
                    if k % 2 == 0:
                        dve.wait_ge(transposed, k + 1)
                        move_chunk(dve.tensor_copy, k).then_inc(xt_dve, 1)

            def cut_lo(i):
                dve.wait_ge(hi_ready, i + 1)
                if i >= 2:
                    dve.wait_ge(looked_up, i - 1)
                dve.tensor_tensor(lo[:, i % 2, :], table[:, i % 2, :], hi[:, i % 2, :].bitcast(F32),
                                  ALU.subtract).then_inc(lo_ready, 1)

            def fold(n):
                dve.wait_ge(z_act, n + 1)
                dve.wait_ge(z_dve, n + 1)
                t, u = divmod(n, UNITS)
                samples = z[:, t % 2].rearrange("p c (q g) -> p c q g", q=QUADS)[:, :, :, u * GPU:(u + 1) * GPU]
                mask = second_sb[:, :, None, None].broadcast_to([P, FOLDS, QUADS, GPU])
                dve.copy_predicated(samples[:, 0:FOLDS], mask, samples[:, FOLDED:PER]).then_inc(folded, 1)

            def move_y(t):
                dve.wait_ge(l3_done, t + 1)
                dve.tensor_copy(y[0:1, t * P:(t + 1) * P].rearrange("p (g q) -> p q g", q=GROUP),
                                l3_row.rearrange("p (q g) -> p q g", q=GROUP)).then_inc(y_dve, 1)

            half = BATCH // 2
            dve.memset(xt[:, 0:half, VECTORS:ROWS], 0.0).then_inc(pads_zeroed, 1)
            dve.wait_ge(ident_ready, 1)
            dve.tensor_copy(select[:], ident[0:HOT, 0:HOT, None].broadcast_to([HOT, HOT, HOT_P])).then_inc(select_ready, 1)
            dve.wait_ge(hot_ids_landed, 16)
            dve.tensor_copy(hot_ids_r[:], hot_ids_sb[:]).then_inc(hot_ids_ready, 1)
            dve.wait_ge(codes_landed, 16)
            for i in range(HOT):
                dve.wait_ge(ids_spread, i + 1)
                if i >= 2:
                    dve.wait_ge(looked_up, i - 1)
                for c in range(HOT_DVE):
                    if i == 0 and c == 2:
                        cut_lo(0)
                    dve.tensor_scalar(onehot[:, i % 2, c, :], ps_g[0:HOT_P, 0, i % 2, :], codes_sb[:, 0, c:c + 1],
                                      None, ALU.is_equal).then_inc(hot_dve, 1)
                if i + 1 < HOT:
                    cut_lo(i + 1)
                move_chunks(range(i - 1, i) if i else ())
            dve.memset(xt[:, half:BATCH, VECTORS:ROWS], 0.0).then_inc(pads_zeroed, 1)
            move_chunks(range(HOT - 1, HOT))
            for t in range(TILES):
                for n in range(t * UNITS, (t + 1) * UNITS):
                    if n == 1:
                        dve.wait_ge(second_landed, 16)
                    if n % UNITS >= 1:
                        fold(n - 1)
                    dve.wait_ge(gram_done, n + 1)
                    move_gram(dve.tensor_copy, n, (0, 1)).then_inc(z_dve, 1)
                    if n % UNITS == UNITS - 1:
                        fold(n)
                    if n % UNITS == 0 and t >= 1:
                        move_y(t - 1)
                    move_chunks(transposes_after(t, f"unit {n % UNITS}"))
                if t == 0:
                    dve.wait_ge(biases_landed, 32)
                for n in range(0, N1, 2):
                    dve.wait_ge(l1_done, t * N1 + n + 1)
                    dve.tensor_scalar(h1[:, n, :], l1_block(n), b1_sb[:, n:n + 1], 0.0,
                                      ALU.add, ALU.max).then_inc(h1_dve, 1)
                move_chunks(transposes_after(t, "layer 1"))
                move_chunks(transposes_after(t, "layer 2"))
            move_y(TILES - 1)

        @block.scalar
        def _(act):
            def move_chunks(chunks):
                for k in chunks:
                    if k % 2 == 1:
                        act.wait_ge(transposed, k + 1)
                        move_chunk(act.copy, k).then_inc(xt_act, 1)

            def cut_hi(i):
                act.wait_ge(table_landed[i % 2], 32 * (i // 2 + 1))
                if i >= 2:
                    act.wait_ge(looked_up, i - 1)
                act.copy(hi[:, i % 2, :], table[:, i % 2, :]).then_inc(hi_ready, 1)

            def move_hot(i):
                act.wait_ge(looked_up, i + 1)
                act.copy(xt[:, :, FIRST_HOT + i], ps_m[:, i % 2, :]).then_inc(xt_hot, 1)

            act.dma_start(ids_sb[:], ids).then_inc(ids_landed, 16)
            act.dma_start(codes_sb[:], codes).then_inc(codes_landed, 16)
            cut_hi(0)
            act.wait_ge(codes_landed, 16)
            for i in range(HOT):
                act.wait_ge(ids_spread, i + 1)
                if i >= 2:
                    act.wait_ge(looked_up, i - 1)
                if i >= 1:
                    act.wait_ge(hot_act, i * HOT_ACT)
                made = i * HOT_ACT
                for c in range(HOT_ACT + 1):
                    if c < HOT_ACT:
                        if c >= 2:
                            act.wait_ge(hot_act, made + c - 1)
                        act.activation(distance[:, c % 2, :], ps_g[0:HOT_P, 1, i % 2, :], ACT.Abs,
                                       bias=codes_sb[:, 1, HOT_DVE + c:HOT_DVE + c + 1]).then_inc(distances, 1)
                    if c >= 1:
                        act.wait_ge(distances, made + c)
                        act.activation(onehot[:, i % 2, HOT_DVE + c - 1, :], distance[:, (c - 1) % 2, :], ACT.Relu,
                                       scale=-1.0, bias=1.0).then_inc(hot_act, 1)
                if i >= 1:
                    move_hot(i - 1)
                if i + 1 < HOT:
                    cut_hi(i + 1)
                move_chunks(range(i - 1, i) if i else ())
            move_hot(HOT - 1)
            move_chunks(range(HOT - 1, HOT))
            for t in range(TILES):
                for n in range(t * UNITS, (t + 1) * UNITS):
                    act.wait_ge(gram_done, n + 1)
                    move_gram(act.copy, n, (2, 3)).then_inc(z_act, 1)
                    move_chunks(transposes_after(t, f"unit {n % UNITS}"))
                if t == 0:
                    act.wait_ge(biases_landed, 32)
                for n in range(1, N1, 2):
                    act.wait_ge(l1_done, t * N1 + n + 1)
                    act.activation(h1[:, n, :], l1_block(n), ACT.Relu, bias=b1_sb[:, n:n + 1]).then_inc(h1_act, 1)
                move_chunks(transposes_after(t, "layer 1"))
                for m in range(N2):
                    act.wait_ge(l2_done, t * N2 + m + 1)
                    act.activation(h2[:, m, :], l2_block(m), ACT.Relu, bias=b2_sb[:, m:m + 1]).then_inc(h2_act, 1)
                move_chunks(transposes_after(t, "layer 2"))


def kernel(**inputs):
    import numpy as np
    import concourse.bacc as bacc
    from concourse.bass_utils import run_bass_kernel_spmd

    gathered, hot = slot_tables([inputs[f"tbl_{f}"].shape[0] for f in range(TABLES)])
    vector_of_slot = [TABLES] + gathered + hot
    ids = np.asarray(inputs["ids"])
    w1 = np.asarray(inputs["W_top1"])
    pairs = VECTORS * (VECTORS - 1) // 2
    labels = labels_of_slots()
    w1_pairs = np.zeros((P, FOLDED, H1), w1.dtype)
    second = np.zeros((P, FOLDS), np.int32)
    for column in range(VECTORS):
        r, c = divmod(column, PER)
        for i in range(VECTORS):
            if takes(labels, i, column):
                w1_pairs[ROWS * r + i, c % FOLDED] = w1[pair_row(vector_of_slot[column], vector_of_slot[i])]
                if c >= FOLDED:
                    second[ROWS * r + i, c - FOLDED] = 1
    row_numbers = np.arange(HOT_ROWS, dtype=np.float32).reshape(HOT_P, HOT_CHUNKS)
    arrays = {
        "r_dense_x": np.asarray(inputs["r_dense_x"]),
        "ids": ids[:, gathered].reshape(TILES, P, GATHERED).transpose(1, 0, 2),
        "hot_ids": ids[:, hot].T,
        "codes": np.stack([row_numbers, -row_numbers], axis=1),
        **{f"tbl_{f}": np.asarray(inputs[f"tbl_{f}"]) for f in range(TABLES)},
        "second": second,
        "w1_pairs": w1_pairs,
        "w1_dense": w1[pairs:],
        "w2": np.asarray(inputs["W_top2"]),
        "w3": np.asarray(inputs["W_top3"]).reshape(N2, P).T,
        "b1": np.asarray(inputs["b_top1"]).reshape(N1, P).T,
        "b2": np.asarray(inputs["b_top2"]).reshape(N2, P).T,
    }
    arrays = {f"{name}_dram": np.ascontiguousarray(a) for name, a in arrays.items()}

    nc = bacc.Bacc("TRN2", target_bir_lowering=False, num_devices=1)
    aps = {name: nc.dram_tensor(name, a.shape, mybir.dt.from_np(a.dtype), kind="ExternalInput").ap()
           for name, a in arrays.items()}
    out = nc.dram_tensor("out_dram", (1, BATCH), F32, kind="ExternalOutput").ap()
    build(nc, aps["r_dense_x_dram"], aps["ids_dram"], aps["hot_ids_dram"], aps["codes_dram"], aps["second_dram"],
          [aps[f"tbl_{f}_dram"] for f in gathered], [aps[f"tbl_{f}_dram"] for f in hot],
          aps["w1_pairs_dram"], aps["w1_dense_dram"], aps["w2_dram"], aps["w3_dram"],
          aps["b1_dram"], aps["b2_dram"], out)
    result = run_bass_kernel_spmd(nc, [arrays], core_ids=[0])
    return result.results[0]["out_dram"].reshape(BATCH, 1)
```

```python
from contextlib import ExitStack

import concourse.bass as bass
from concourse import mybir

F32 = mybir.dt.float32
F32R = mybir.dt.float32r
I32 = mybir.dt.int32
ALU = mybir.AluOpType
ACT = mybir.ActivationFunctionType

P = 128
D = 128
BATCH = 512
TABLES = 26
VECTORS = TABLES + 1
HOT_ROWS = 1000
HOT = 7
HOT_CHUNKS = 8
HOT_P = HOT_ROWS // HOT_CHUNKS
HOT_DVE = 5
HOT_ACT = HOT_CHUNKS - HOT_DVE
HOT_DVE_STEPS = ((0, 2), (2, HOT_DVE))
GATHERED = TABLES - HOT
DENSE = 0
FIRST_HOT = 1 + GATHERED
WARM_UP = (6, 5)
TILES = BATCH // P
QUADS = 4
ROWS = P // QUADS
PER = -(-VECTORS // QUADS)
COLS = PER * QUADS
FOLDS = PER // 2
FOLDED = PER - FOLDS
GROUP = QUADS
GRAM_ROWS = (GROUP - 1) * ROWS + VECTORS
GROUPS = P // GROUP
BANK = 512
GPB = BANK // (GROUP * COLS)
UNIT_BANKS = 2
GPU = GPB * UNIT_BANKS
UNITS = GROUPS // GPU
CHUNK = BANK // P
CHUNK_STARTS = (*range(0, FIRST_HOT - 2, CHUNK), FIRST_HOT - 2, FIRST_HOT)
CHUNKS = len(CHUNK_STARTS) - 1
EARLY = CHUNKS + 2
TRANSPOSES = ((0, 1, 2, 4, 4, 4), (0, 1, 2, 4, 6, 6), (0, 1, 2, 3, 4, 6))
H1, H2 = 512, 256
N1, N2 = H1 // P, H2 // P
L2_ORDER = (0, 2, 1, 3)


def pair_row(i, j):
    i, j = min(i, j), max(i, j)
    return i * VECTORS - i * (i + 1) // 2 + j - i - 1


def labels_of_slots():
    labels, firsts, half = {}, 0, VECTORS // 2
    for r in range(QUADS):
        for c in range(FOLDS):
            first, second = PER * r + c, PER * r + c + FOLDED
            if second < VECTORS:
                labels[first], labels[second] = firsts, firsts + half
                firsts += 1
    others = [x for x in range(VECTORS) if x not in labels.values()]
    for s in range(VECTORS):
        if s not in labels:
            labels[s] = others.pop(0)
    return labels


def takes(labels, row, column):
    return column < VECTORS and 1 <= (labels[column] - labels[row]) % VECTORS <= VECTORS // 2


def slot_tables(row_counts):
    hot = [f for f, rows in enumerate(row_counts) if rows == HOT_ROWS][:HOT]
    return [f for f in range(TABLES) if f not in hot], hot


def build(nc, r_dense_x, ids, hot_ids, codes, second, gathered_tables, hot_tables, w1_pairs, w1_dense, w2, w3, b1, b2, out):
    with ExitStack() as ctx:
        def sb(name, shape, dt=F32):
            return ctx.enter_context(nc.sbuf_tensor(name, shape, dt))

        def psum(name, shape):
            return ctx.enter_context(nc.psum_tensor(name, shape, F32))

        def sem(name):
            return ctx.enter_context(nc.semaphore(name))

        ids_sb = sb("ids_sb", [P, TILES, GATHERED], I32)
        hot_ids_sb = sb("hot_ids_sb", [HOT, BATCH], I32)
        hot_ids_r = sb("hot_ids_r", [P, BATCH], F32R)
        select = sb("select", [P, HOT, HOT_P], F32R)
        codes_sb = sb("codes_sb", [HOT_P, 2, HOT_CHUNKS])
        table = sb("table", [HOT_P, 2, HOT_CHUNKS * D])
        hi = sb("hi", [HOT_P, 2, HOT_CHUNKS * D], F32R)
        lo = sb("lo", [HOT_P, 2, HOT_CHUNKS * D], F32R)
        onehot = sb("onehot", [HOT_P, 2, HOT_CHUNKS, BATCH], F32R)
        distance = sb("distance", [HOT_P, HOT_ACT, BATCH])
        rows = sb("rows", [P, TILES, FIRST_HOT, D])
        xt = sb("xt", [P, BATCH, ROWS])
        z = sb("z", [P, 2, PER, P])
        second_sb = sb("second_sb", [P, FOLDS], I32)
        w1p_sb = sb("w1p_sb", [P, FOLDED, H1])
        w1d_sb = sb("w1d_sb", [P, H1])
        w2_sb = sb("w2_sb", [P, N1, H2])
        w3_sb = sb("w3_sb", [P, N2])
        b1_sb = sb("b1_sb", [P, N1])
        b2_sb = sb("b2_sb", [P, N2])
        h1 = sb("h1", [P, N1, P])
        h2 = sb("h2", [P, N2, P])
        y = sb("y", [1, BATCH])
        ident = sb("ident", [P, P])

        ps_t = psum("ps_t", [P, 2, BANK])
        ps_g = psum("ps_g", [P, 2, UNIT_BANKS, BANK])
        ps_m = psum("ps_m", [P, 2, BANK])

        ids_landed = sem("ids_landed")
        hot_ids_landed = sem("hot_ids_landed")
        codes_landed = sem("codes_landed")
        table_landed = [sem(f"table_landed_{i}") for i in range(2)]
        hot_ids_ready = sem("hot_ids_ready")
        hot_ids_zeroed = sem("hot_ids_zeroed")
        select_ready = sem("select_ready")
        hi_ready = sem("hi_ready")
        lo_ready = sem("lo_ready")
        ids_spread = sem("ids_spread")
        hot_dve = sem("hot_dve")
        hot_act = sem("hot_act")
        distances = sem("distances")
        looked_up = sem("looked_up")
        hot_xt_act = sem("hot_xt_act")
        hot_xt_dve = sem("hot_xt_dve")
        dense_landed = sem("dense_landed")
        w1_landed = sem("w1_landed")
        w23_landed = sem("w23_landed")
        biases_landed = sem("biases_landed")
        second_landed = sem("second_landed")
        rows_landed = [[sem(f"rows_landed_{t}_{c}") for c in range(CHUNKS)] for t in range(TILES)]
        ident_zeroed = sem("ident_zeroed")
        h2_zeroed = sem("h2_zeroed")
        ident_ready = sem("ident_ready")
        pads_zeroed = sem("pads_zeroed")
        z_zeroed = sem("z_zeroed")
        transposed = sem("transposed")
        xt_dve = sem("xt_dve")
        xt_act = sem("xt_act")
        gram_done = sem("gram_done")
        z_dve = sem("z_dve")
        z_act = sem("z_act")
        folded = sem("folded")
        l1_done = sem("l1_done")
        h1_dve = sem("h1_dve")
        h1_act = sem("h1_act")
        l2_done = sem("l2_done")
        h2_act = sem("h2_act")
        l3_done = sem("l3_done")
        y_dve = sem("y_dve")
        y_stored = sem("y_stored")

        def chunk_slots(c):
            return range(CHUNK_STARTS[c], CHUNK_STARTS[c + 1])

        def chunks_before(t, parity):
            return len([k for k in range(t * CHUNKS) if k % 2 == parity])

        def move_chunk(copy, k):
            t, c = divmod(k, CHUNKS)
            s = chunk_slots(c)
            src = ps_t[:, k % 2, 0:len(s) * P].rearrange("d (s b) -> d b s", b=P)
            return copy(xt[:, t * P:(t + 1) * P, s.start:s.stop], src)

        def move_hot(copy, i):
            return copy(xt[:, :, FIRST_HOT + i], ps_m[:, i % 2, :])

        def move_gram(copy, n, quads):
            t, u = divmod(n, UNITS)
            for q in quads:
                width = VECTORS if q == QUADS - 1 else ROWS
                for r in range(QUADS):
                    src = ps_g[ROWS * q:ROWS * q + width, n % 2, :, 0:GPB * GROUP * COLS].rearrange(
                        "p k (g m) -> p k g m", g=GPB)[:, :, :, q * COLS + r * PER:q * COLS + (r + 1) * PER]
                    first = q * GROUPS + u * GPU
                    dst = z[ROWS * r:ROWS * r + width, t % 2, :, first:first + GPU].rearrange("p c (k g) -> p k g c", k=UNIT_BANKS)
                    last = copy(dst, src)
            return last

        def l1_block(n):
            return ps_m[:, n, 0:P] if n < 2 else ps_g[:, 0, n - 2, 0:P]

        def l2_block(m):
            return ps_m[:, m, P:2 * P]

        l3_row = ps_m[0:1, 0, BANK - P:BANK]

        def transposes_after(t, step):
            chunks = range(max((t + 1) * CHUNKS, EARLY), min((t + 2) * CHUNKS, TILES * CHUNKS))
            steps = ("unit 0", "unit 1", "unit 2", "unit 3", "layer 1", "layer 2")
            ends = TRANSPOSES[t] if t < len(TRANSPOSES) else (0,) * len(steps)
            at = steps.index(step)
            return chunks[ends[at - 1] if at else 0:ends[at]]

        block = ctx.enter_context(nc.Block())

        @block.sync
        def _(sp):
            def load_table(i):
                src = hot_tables[i].rearrange("(p c) d -> p (c d)", c=HOT_CHUNKS)
                if i >= 2:
                    sp.wait_ge(lo_ready, i - 1)
                whole = HOT_P // 16 * 16
                sp.dma_start(table[0:whole, i % 2, :], src[0:whole]).then_inc(table_landed[i % 2], 16)
                sp.dma_start(table[whole:HOT_P, i % 2, :], src[whole:HOT_P]).then_inc(table_landed[i % 2], 16)

            sp.dma_start(ids_sb[:], ids).then_inc(ids_landed, 16)
            sp.dma_start(codes_sb[:], codes).then_inc(codes_landed, 16)
            load_table(0)
            load_table(1)
            sp.dma_start(rows[:, :, DENSE, :], r_dense_x.rearrange("(t p) d -> p t d", p=P)).then_inc(dense_landed, 16)
            for i in range(2, HOT):
                load_table(i)
            sp.dma_start(second_sb[:], second).then_inc(second_landed, 16)
            sp.dma_start(w1d_sb[:], w1_dense).then_inc(w1_landed, 16)
            sp.dma_start(w1p_sb[:], w1_pairs).then_inc(w1_landed, 16)
            sp.dma_start(w2_sb[:], w2.rearrange("(k p) n -> p k n", p=P)).then_inc(w23_landed, 16)
            sp.dma_start(w3_sb[:], w3).then_inc(w23_landed, 16)
            sp.dma_start(b1_sb[:], b1).then_inc(biases_landed, 16)
            sp.dma_start(b2_sb[:], b2).then_inc(biases_landed, 16)
            sp.wait_ge(y_dve, TILES)
            sp.dma_start(out, y[:]).then_inc(y_stored, 16)
            sp.wait_ge(y_stored, 16)

        @block.gpsimd
        def _(pool):
            pool.memset(ident[:], 0.0).then_inc(ident_zeroed, 1)
            pool.wait_ge(ident_zeroed, 1)
            pool.affine_select(out=ident[:], in_=ident[:], compare_op=ALU.not_equal, fill=1.0, base=0,
                               pattern=[[-1, P]], channel_multiplier=1).then_inc(ident_ready, 1)
            pool.memset(xt[:, 0:BATCH // 2, VECTORS:ROWS], 0.0).then_inc(pads_zeroed, 1)
            pool.wait_ge(ids_landed, 16)
            for t in range(TILES):
                for c in range(CHUNKS):
                    for f in chunk_slots(c):
                        if f != DENSE:
                            pool.indirect_dma_start(
                                out=rows[:, t, f, :], out_offset=None, in_=gathered_tables[f - 1],
                                in_offset=bass.IndirectOffsetOnAxis(ap=ids_sb[:, t, f - 1:f], axis=0),
                            ).then_inc(rows_landed[t][c], 16)

        @block.tensor
        def _(pe):
            vectors = xt[:].rearrange("d b s -> d (b s)")

            def warm_up(products):
                for _ in range(products):
                    pe.matmul(ps_t[:, 0, 0:P], h2[:, 0, :], h2[:, 1, :], start=True, stop=True)

            def spread_ids(i):
                for e in (1, 0):
                    pe.matmul(ps_g[0:HOT_P, e, i % 2, :], select[:, i, :], hot_ids_r[:],
                              start=True, stop=True).then_inc(ids_spread, 1)

            def look_up(i):
                pe.wait_ge(hi_ready, i + 1)
                if i >= 2:
                    pe.wait_ge(hot_xt_dve if i % 2 else hot_xt_act, i // 2)
                for half in (hi, lo):
                    if half is lo:
                        pe.wait_ge(lo_ready, i + 1)
                    for c in range(HOT_CHUNKS):
                        if half is hi and c == 0:
                            pe.wait_ge(hot_dve, i * 2 + 1)
                        if half is hi and c == HOT_DVE_STEPS[1][0]:
                            pe.wait_ge(hot_dve, i * 2 + 2)
                        if half is hi and c == HOT_DVE:
                            pe.wait_ge(hot_act, i + 1)
                        last = pe.matmul(ps_m[:, i % 2, :], half[:, i % 2, c * D:(c + 1) * D], onehot[:, i % 2, c, :],
                                         start=(half is hi and c == 0), stop=(half is lo and c == HOT_CHUNKS - 1))
                last.then_inc(looked_up, 1)

            def layer_3(t):
                for m in range(N2):
                    pe.wait_ge(h2_act, t * N2 + m + 1)
                    last = pe.matmul(l3_row, w3_sb[:, m:m + 1], h2[:, m, :],
                                     start=(m == 0), stop=(m == N2 - 1))
                last.then_inc(l3_done, 1)

            def transpose_chunk(k):
                t, c = divmod(k, CHUNKS)
                s = chunk_slots(c)
                pe.wait_ge(rows_landed[t][c], 16 * len([f for f in s if f != DENSE]))
                if DENSE in s:
                    pe.wait_ge(dense_landed, 16)
                if k >= 2:
                    pe.wait_ge(xt_act if k % 2 else xt_dve, k // 2)
                for i, f in enumerate(s):
                    last = pe.transpose(ps_t[:, k % 2, i * P:(i + 1) * P], rows[:, t, f, :], ident[:])
                last.then_inc(transposed, 1)

            pe.wait_ge(h2_zeroed, 1)
            warm_up(WARM_UP[0])
            pe.wait_ge(hot_ids_ready, 1)
            pe.wait_ge(select_ready, 1)
            spread_ids(0)
            warm_up(WARM_UP[1])
            spread_ids(1)
            for i in range(HOT):
                look_up(i)
                if i + 2 < HOT:
                    spread_ids(i + 2)
                if i == 0:
                    pe.wait_ge(ident_ready, 1)
                if i < CHUNKS:
                    transpose_chunk(i)
            for k in range(CHUNKS, EARLY):
                transpose_chunk(k)
            for t in range(TILES):
                if t == TILES - 1:
                    layer_3(t - 1)
                if t % (TILES // 2) == 0:
                    pe.wait_ge(pads_zeroed, 1 + t // (TILES // 2))
                if t == 0:
                    pe.wait_ge(hot_xt_act, (HOT + 1) // 2)
                    pe.wait_ge(hot_xt_dve, HOT // 2)
                pe.wait_ge(xt_dve, chunks_before(t + 1, 0))
                pe.wait_ge(xt_act, chunks_before(t + 1, 1))
                for u in range(UNITS):
                    n = t * UNITS + u
                    if n >= 2:
                        pe.wait_ge(z_dve, n - 1)
                        pe.wait_ge(z_act, n - 1)
                    for g in range(GPU):
                        b = t * P + (u * GPU + g) * GROUP
                        at = (g % GPB) * GROUP * COLS
                        last = pe.matmul(ps_g[0:GRAM_ROWS, n % 2, g // GPB, at:at + GROUP * COLS],
                                         vectors[:, b * ROWS:b * ROWS + GRAM_ROWS], xt[:, b:b + GROUP, 0:COLS], start=True, stop=True)
                    last.then_inc(gram_done, 1)
                    if u == 0 and 1 <= t < TILES - 1:
                        layer_3(t - 1)
                    for k in transposes_after(t, f"unit {u}"):
                        transpose_chunk(k)
                if t == 0:
                    pe.wait_ge(w1_landed, 32)
                if t >= 1:
                    pe.wait_ge(h2_act, t * N2)
                    pe.wait_ge(y_dve, t)
                dense = xt[:, t * P:(t + 1) * P, DENSE].rearrange("d (g q) -> d q g", q=GROUP)

                def pairs(n, c):
                    return pe.matmul(l1_block(n), w1p_sb[:, c, n * P:(n + 1) * P], z[:, t % 2, c, :],
                                     start=False, stop=(c == FOLDS - 1))

                pe.wait_ge(z_dve, (t + 1) * UNITS - 1)
                pe.wait_ge(z_act, (t + 1) * UNITS - 1)
                for n in range(N1):
                    pe.matmul(l1_block(n), w1d_sb[:, n * P:(n + 1) * P], dense, start=True, stop=False)
                pe.wait_ge(z_dve, (t + 1) * UNITS)
                pe.wait_ge(z_act, (t + 1) * UNITS)
                for n in range(N1):
                    for c in range(FOLDS, FOLDED):
                        pairs(n, c)
                pe.wait_ge(folded, (t + 1) * UNITS)
                for n in range(N1):
                    for c in range(FOLDS):
                        last = pairs(n, c)
                    last.then_inc(l1_done, 1)
                for k in transposes_after(t, "layer 1"):
                    transpose_chunk(k)
                if t == 0:
                    pe.wait_ge(w23_landed, 32)
                pe.wait_ge(h1_dve, (t + 1) * 2)
                for m in range(N2):
                    for n in L2_ORDER:
                        if m == 0 and n % 2:
                            pe.wait_ge(h1_act, t * 2 + n // 2 + 1)
                        last = pe.matmul(l2_block(m), w2_sb[:, n, m * P:(m + 1) * P],
                                         h1[:, n, :], start=(n == 0), stop=(n == L2_ORDER[-1]))
                    last.then_inc(l2_done, 1)
                for k in transposes_after(t, "layer 2"):
                    transpose_chunk(k)
            layer_3(TILES - 1)

        @block.vector
        def _(dve):
            def move_chunks(chunks):
                for k in chunks:
                    if k % 2 == 0:
                        dve.wait_ge(transposed, k + 1)
                        move_chunk(dve.tensor_copy, k).then_inc(xt_dve, 1)

            def cut_lo(i):
                dve.wait_ge(hi_ready, i + 1)
                if i >= 2:
                    dve.wait_ge(looked_up, i - 1)
                dve.tensor_tensor(lo[:, i % 2, :], table[:, i % 2, :], hi[:, i % 2, :].bitcast(F32),
                                  ALU.subtract).then_inc(lo_ready, 1)

            def fold(n):
                dve.wait_ge(z_act, n + 1)
                dve.wait_ge(z_dve, n + 1)
                t, u = divmod(n, UNITS)
                samples = z[:, t % 2].rearrange("p c (q g) -> p c q g", q=QUADS)[:, :, :, u * GPU:(u + 1) * GPU]
                mask = second_sb[:, :, None, None].broadcast_to([P, FOLDS, QUADS, GPU])
                dve.copy_predicated(samples[:, 0:FOLDS], mask, samples[:, FOLDED:PER]).then_inc(folded, 1)

            def move_y(t):
                dve.wait_ge(l3_done, t + 1)
                dve.tensor_copy(y[0:1, t * P:(t + 1) * P].rearrange("p (g q) -> p q g", q=GROUP),
                                l3_row.rearrange("p (q g) -> p q g", q=GROUP)).then_inc(y_dve, 1)

            dve.memset(h2[:], 0.0).then_inc(h2_zeroed, 1)
            dve.memset(hot_ids_r[:].bitcast(F32), 0.0).then_inc(hot_ids_zeroed, 1)
            dve.wait_ge(ident_ready, 1)
            dve.tensor_copy(select[:], ident[:, 0:HOT, None].broadcast_to([P, HOT, HOT_P])).then_inc(select_ready, 1)
            dve.memset(z[:, :, :, (QUADS - 1) * GROUPS:P], 0.0).then_inc(z_zeroed, 1)
            dve.wait_ge(hot_ids_landed, 16)
            dve.wait_ge(hot_ids_zeroed, 1)
            dve.tensor_copy(hot_ids_r[0:HOT, :], hot_ids_sb[:]).then_inc(hot_ids_ready, 1)
            dve.wait_ge(codes_landed, 16)
            for i in range(HOT):
                dve.wait_ge(ids_spread, 2 * i + 2)
                if i >= 2:
                    dve.wait_ge(looked_up, i - 1)
                for first, end in HOT_DVE_STEPS:
                    shape = [HOT_P, end - first, BATCH]
                    dve.tensor_tensor(onehot[:, i % 2, first:end, :], ps_g[0:HOT_P, 0, i % 2, None, :].broadcast_to(shape),
                                      codes_sb[:, 0, first:end, None].broadcast_to(shape),
                                      ALU.is_equal).then_inc(hot_dve, 1)
                cut_lo(i)
                if i >= 2 and i % 2 == 0:
                    dve.wait_ge(looked_up, i)
                    move_hot(dve.tensor_copy, i - 1).then_inc(hot_xt_dve, 1)
                move_chunks(range(i - 1, i) if i else ())
            if (HOT - 1) % 2:
                dve.wait_ge(looked_up, HOT)
                move_hot(dve.tensor_copy, HOT - 1).then_inc(hot_xt_dve, 1)
            move_chunks(range(CHUNKS, EARLY))
            for t in range(TILES):
                if t == TILES - 1:
                    move_y(t - 1)
                for n in range(t * UNITS, (t + 1) * UNITS):
                    if n == 1:
                        dve.wait_ge(second_landed, 16)
                    if n % UNITS >= 1:
                        fold(n - 1)
                    dve.wait_ge(gram_done, n + 1)
                    if n == 0:
                        dve.wait_ge(z_zeroed, 1)
                    move_gram(dve.tensor_copy, n, (0, 1)).then_inc(z_dve, 1)
                    if n % UNITS == UNITS - 1:
                        fold(n)
                    if n % UNITS == 0 and 1 <= t < TILES - 1:
                        move_y(t - 1)
                    move_chunks(transposes_after(t, f"unit {n % UNITS}"))
                if t == 0:
                    dve.memset(xt[:, BATCH // 2:BATCH, VECTORS:ROWS], 0.0).then_inc(pads_zeroed, 1)
                    dve.wait_ge(biases_landed, 32)
                for n in range(0, N1, 2):
                    dve.wait_ge(l1_done, t * N1 + n + 1)
                    dve.tensor_scalar(h1[:, n, :], l1_block(n), b1_sb[:, n:n + 1], 0.0,
                                      ALU.add, ALU.max).then_inc(h1_dve, 1)
                move_chunks(transposes_after(t, "layer 1"))
                move_chunks(transposes_after(t, "layer 2"))
            move_y(TILES - 1)

        @block.scalar
        def _(act):
            def move_chunks(chunks):
                for k in chunks:
                    if k % 2 == 1:
                        act.wait_ge(transposed, k + 1)
                        move_chunk(act.copy, k).then_inc(xt_act, 1)

            def cut_hi(i):
                act.wait_ge(table_landed[i % 2], 32 * (i // 2 + 1))
                if i >= 2:
                    act.wait_ge(looked_up, i - 1)
                act.copy(hi[:, i % 2, :], table[:, i % 2, :]).then_inc(hi_ready, 1)

            act.dma_start(hot_ids_sb[:], hot_ids).then_inc(hot_ids_landed, 16)
            act.wait_ge(h2_zeroed, 1)
            act.activation(h1[:, 0, 0:1], h2[:, 0, 0:1], ACT.Abs)
            act.wait_ge(codes_landed, 16)
            for i in range(HOT):
                act.wait_ge(ids_spread, 2 * i + 1)
                if i >= 2:
                    act.wait_ge(looked_up, i - 1)
                if i >= 1:
                    act.wait_ge(hot_act, i)
                for c in range(HOT_ACT):
                    last = act.activation(distance[:, c, :], ps_g[0:HOT_P, 1, i % 2, :], ACT.Abs,
                                          bias=codes_sb[:, 1, HOT_DVE + c:HOT_DVE + c + 1])
                last.then_inc(distances, 1)
                cut_hi(i)
                act.wait_ge(distances, i + 1)
                act.activation(onehot[:, i % 2, HOT_DVE:HOT_CHUNKS, :], distance[:], ACT.Relu,
                               scale=-1.0, bias=1.0).then_inc(hot_act, 1)
                if i % 2:
                    act.wait_ge(looked_up, i)
                    move_hot(act.copy, i - 1).then_inc(hot_xt_act, 1)
                move_chunks(range(i - 1, i) if i else ())
            if (HOT - 1) % 2 == 0:
                act.wait_ge(looked_up, HOT)
                move_hot(act.copy, HOT - 1).then_inc(hot_xt_act, 1)
            move_chunks(range(CHUNKS, EARLY))
            for t in range(TILES):
                for n in range(t * UNITS, (t + 1) * UNITS):
                    act.wait_ge(gram_done, n + 1)
                    if n == 0:
                        act.wait_ge(z_zeroed, 1)
                    move_gram(act.copy, n, (2, 3)).then_inc(z_act, 1)
                    move_chunks(transposes_after(t, f"unit {n % UNITS}"))
                if t == 0:
                    act.wait_ge(biases_landed, 32)
                for n in range(1, N1, 2):
                    act.wait_ge(l1_done, t * N1 + n + 1)
                    act.activation(h1[:, n, :], l1_block(n), ACT.Relu, bias=b1_sb[:, n:n + 1]).then_inc(h1_act, 1)
                move_chunks(transposes_after(t, "layer 1"))
                for m in range(N2):
                    act.wait_ge(l2_done, t * N2 + m + 1)
                    act.activation(h2[:, m, :], l2_block(m), ACT.Relu, bias=b2_sb[:, m:m + 1]).then_inc(h2_act, 1)
                move_chunks(transposes_after(t, "layer 2"))


def kernel(**inputs):
    import numpy as np
    import concourse.bacc as bacc
    from concourse.bass_utils import run_bass_kernel_spmd

    gathered, hot = slot_tables([inputs[f"tbl_{f}"].shape[0] for f in range(TABLES)])
    vector_of_slot = [TABLES] + gathered + hot
    ids = np.asarray(inputs["ids"])
    w1 = np.asarray(inputs["W_top1"])
    pairs = VECTORS * (VECTORS - 1) // 2
    labels = labels_of_slots()
    w1_pairs = np.zeros((P, FOLDED, H1), w1.dtype)
    second = np.zeros((P, FOLDS), np.int32)
    for column in range(VECTORS):
        r, c = divmod(column, PER)
        for i in range(VECTORS):
            if takes(labels, i, column):
                w1_pairs[ROWS * r + i, c % FOLDED] = w1[pair_row(vector_of_slot[column], vector_of_slot[i])]
                if c >= FOLDED:
                    second[ROWS * r + i, c - FOLDED] = 1
    row_numbers = np.arange(HOT_ROWS, dtype=np.float32).reshape(HOT_P, HOT_CHUNKS)
    arrays = {
        "r_dense_x": np.asarray(inputs["r_dense_x"]),
        "ids": ids[:, gathered].reshape(TILES, P, GATHERED).transpose(1, 0, 2),
        "hot_ids": ids[:, hot].T,
        "codes": np.stack([row_numbers, -row_numbers], axis=1),
        **{f"tbl_{f}": np.asarray(inputs[f"tbl_{f}"]) for f in range(TABLES)},
        "second": second,
        "w1_pairs": w1_pairs,
        "w1_dense": w1[pairs:],
        "w2": np.asarray(inputs["W_top2"]),
        "w3": np.asarray(inputs["W_top3"]).reshape(N2, P).T,
        "b1": np.asarray(inputs["b_top1"]).reshape(N1, P).T,
        "b2": np.asarray(inputs["b_top2"]).reshape(N2, P).T,
    }
    arrays = {f"{name}_dram": np.ascontiguousarray(a) for name, a in arrays.items()}

    nc = bacc.Bacc("TRN2", target_bir_lowering=False, num_devices=1)
    aps = {name: nc.dram_tensor(name, a.shape, mybir.dt.from_np(a.dtype), kind="ExternalInput").ap()
           for name, a in arrays.items()}
    out = nc.dram_tensor("out_dram", (1, BATCH), F32, kind="ExternalOutput").ap()
    build(nc, aps["r_dense_x_dram"], aps["ids_dram"], aps["hot_ids_dram"], aps["codes_dram"], aps["second_dram"],
          [aps[f"tbl_{f}_dram"] for f in gathered], [aps[f"tbl_{f}_dram"] for f in hot],
          aps["w1_pairs_dram"], aps["w1_dense_dram"], aps["w2_dram"], aps["w3_dram"],
          aps["b1_dram"], aps["b2_dram"], out)
    result = run_bass_kernel_spmd(nc, [arrays], core_ids=[0])
    return result.results[0]["out_dram"].reshape(BATCH, 1)
```
